# Optimizing a Trainium2 kernel written in Bass

```python
import numpy as np
import jax
import jax.numpy as jnp

def _softmax(x, axis=-1):
    return jax.nn.softmax(x, axis=axis)

def _gelu(x):
    return jax.nn.gelu(x, approximate=True)

def _silu(x):
    return jax.nn.silu(x)

def _sigmoid(x):
    return jax.nn.sigmoid(x)

def _layernorm(x, axis=-1, eps=1e-05):
    m = jnp.mean(x, axis=axis, keepdims=True)
    v = jnp.var(x, axis=axis, keepdims=True)
    return (x - m) / jnp.sqrt(v + eps)

def _scatter_add(tgt, idx, src, axis=0):
    return tgt.at[idx].add(src)

def _segment_sum(src, seg, n):
    return jax.ops.segment_sum(src, seg, n)
kernel_name = 'mk_adj_preln_d1_adj_r2_bb32ed'

def setup_inputs(seed: int=0):
    np.random.seed(seed)
    _w = jnp.asarray

    def _rec_inputs():
        import jax
        import jax.numpy as jnp
        _gk = jax.random.key(seed)
        x = -8.776e-05 + 1 * jax.random.normal(jax.random.fold_in(_gk, 1), (10000, 128), jnp.float32)
        _a = jax.random.bernoulli(jax.random.fold_in(_gk, 2), 0.0016, (10000, 10000))
        _a = jnp.logical_or(_a, jnp.eye(10000, dtype=bool))
        _af = _a.astype(jnp.float32)
        _af = _af * jax.random.uniform(jax.random.fold_in(_gk, 3), (10000, 10000), jnp.float32, 0.05, 1)
        adj = _af
        return (x, adj)
    x, adj = _rec_inputs()

    def _L0_gnn_setup():
        import jax, jax.numpy as jnp
        import numpy as np
        N_USER = 10000
        N_ITEM = 10000
        HID = 128
        key = jax.random.key(seed)
        k1, k2, k3, k4, k5, k6, k7 = jax.random.split(key, 7)
        scale = 1.0 / np.sqrt(HID)
        return {'user_feat': jax.random.normal(k1, (N_USER, HID), dtype=jnp.float32), 'item_feat': jax.random.normal(k2, (N_ITEM, HID), dtype=jnp.float32), 'adj': jax.random.uniform(k3, (N_USER, N_ITEM), dtype=jnp.float32), 'W_item': jax.random.uniform(k4, (HID, HID), dtype=jnp.float32, minval=-scale, maxval=scale), 'b_item': jax.random.uniform(k5, (HID,), dtype=jnp.float32, minval=-scale, maxval=scale), 'W_user': jax.random.uniform(k6, (HID, HID), dtype=jnp.float32, minval=-scale, maxval=scale), 'b_user': jax.random.uniform(k7, (HID,), dtype=jnp.float32, minval=-scale, maxval=scale)}
    _L0_gnn_all = _L0_gnn_setup()
    _L0_gnn_in = {k: v for k, v in _L0_gnn_all.items() if k in ('item_feat', 'W_item', 'b_item', 'W_user', 'b_user')}
    del _L0_gnn_all
    return {'x': x, 'adj': adj, 'L0_gnn_item_feat': _L0_gnn_in['item_feat'], 'L0_gnn_W_item': _L0_gnn_in['W_item'], 'L0_gnn_b_item': _L0_gnn_in['b_item'], 'L0_gnn_W_user': _L0_gnn_in['W_user'], 'L0_gnn_b_user': _L0_gnn_in['b_user']}

def reference(x, adj, L0_gnn_item_feat, L0_gnn_W_item, L0_gnn_b_item, L0_gnn_W_user, L0_gnn_b_user):
    import jax
    import jax.numpy as jnp

    def _L0_gnn_ref(user_feat, item_feat, adj, W_item, b_item, W_user, b_user):
        import jax, jax.numpy as jnp
        import numpy as np
        N_USER = 10000
        N_ITEM = 10000
        HID = 128
        h = item_feat @ W_item.T + b_item
        b = user_feat @ W_user.T + b_user
        return jax.nn.relu(adj @ h + b)
    h = jnp.maximum(_layernorm(x, axis=-1), 0.0)
    x = x + _L0_gnn_ref(h, L0_gnn_item_feat, adj, L0_gnn_W_item, L0_gnn_b_item, L0_gnn_W_user, L0_gnn_b_user)
    return x

_drawn_inputs = setup_inputs


def setup_inputs(seed=0):
    import zlib

    import numpy as np

    out = dict(_drawn_inputs(seed))
    spreads = {}
    factors = {}
    for name, (base, spread) in spreads.items():
        noise = np.random.default_rng([zlib.crc32(name.encode()), seed]).standard_normal(out[name].shape)
        drawn = base * np.exp(spread * noise) if base else spread * noise
        out[name] = jnp.asarray(drawn.astype(out[name].dtype))
    for name, factor in factors.items():
        out[name] = (out[name] * factor).astype(out[name].dtype)
    return out
```

```python
from contextlib import ExitStack

import concourse.bass as bass
from concourse import mybir

P = 128
N_USER = 10000
N_ITEM = 10000
HID = 128
EPS = 1e-5

GROUPS = 4
ACC_BANKS = 5
GROUP_W = N_USER // GROUPS
BANK_W = GROUP_W // ACC_BANKS
ROW_TILES = 4
ROW_T = BANK_W // ROW_TILES

CHUNKS = N_ITEM // P
REM = N_ITEM - CHUNKS * P
A_SLOTS = 4
S_SLOTS = 3
BODY = A_SLOTS * S_SLOTS
REM_SLOT = CHUNKS % A_SLOTS
LOADS = [len(range(s, CHUNKS, A_SLOTS)) for s in range(A_SLOTS)]
SPLITS = CHUNKS // S_SLOTS

QUAD = 4
QUADS = -(-N_ITEM // (QUAD * P))
H_BANKS = 3
ITEM_Y = 5 * QUAD * P
UNITS = ACC_BANKS
FREE = 1

assert GROUP_W * GROUPS == N_USER and BANK_W * ACC_BANKS == GROUP_W and BANK_W <= 512
assert CHUNKS % S_SLOTS == 0 and N_ITEM <= ITEM_Y + (A_SLOTS - 1) * GROUP_W

F32 = mybir.dt.float32
F32R = mybir.dt.float32r
ALU = mybir.AluOpType
ACT = mybir.ActivationFunctionType
AX_X = mybir.AxisListType.X

CENTRE_AT = 4
SQUARE_AT = 7
VAR_AT = 8
SQRT_AT = 11
NORM_AT = 12
TRANSPOSE_AT = 14
COPY_AT = 17
USER_AT = 18
AHEAD = 2
VECTOR_LOOP_AT = 2
SCALAR_LOOP_AT = 6
EARLY = {12: 0, 16: 1}


def graph_layer(nc, adj_tiles, adj_rem, ones_row, item_t, x_rows, w_item_t, b_item, w_user_t, b_user, out_t):
    with ExitStack() as ctx:
        def sb(name, shape, dt=F32):
            return ctx.enter_context(nc.sbuf_tensor(name, shape, dt))

        def sem(name):
            return ctx.enter_context(nc.semaphore(name))

        a_ring = sb("a_ring", [P, A_SLOTS, GROUP_W])
        hi_ring = sb("hi_ring", [P, S_SLOTS, GROUP_W], F32R)
        lo_ring = sb("lo_ring", [P, S_SLOTS, GROUP_W], F32R)
        h_hi = sb("h_hi", [P, CHUNKS, HID], F32R)
        h_lo = sb("h_lo", [P, CHUNKS, HID], F32R)
        h_rem = sb("h_rem", [REM + 1, HID])
        wi = sb("wi", [P, HID])
        wu = sb("wu", [P, HID])
        bi = sb("bi", [2, HID])
        bi_hi = sb("bi_hi", [2, HID], F32R)
        bi_parts = sb("bi_parts", [2, HID], F32R)
        ones_f = sb("ones_f", [2, P])
        ones_r = sb("ones_r", [2, P], F32R)
        take_hi = sb("take_hi", [2, 1])
        ident = sb("ident", [ROW_T, ROW_T])
        y = sb("y", [P, max(GROUP_W, ITEM_Y)])
        rows = sb("rows", [ROW_T, ROW_TILES, HID])
        centred = sb("centred", [ROW_T, ROW_TILES, HID])
        squares = sb("squares", [ROW_T, ROW_TILES, HID])
        normed = sb("normed", [ROW_T, ROW_TILES, HID])
        normed_t = sb("normed_t", [P, BANK_W])
        stat = sb("stat", [ROW_T, 8, ROW_TILES])
        total, mean, total_sq, var, std, inv, root, rstd = (stat[:, i, :] for i in range(8))

        acc = [ctx.enter_context(nc.psum_tensor(f"acc{k}", [P, 512], F32)) for k in range(ACC_BANKS)]
        spare = [ctx.enter_context(nc.psum_tensor(f"spare{k}", [P, 512], F32)) for k in range(H_BANKS)]
        turned, turned_x = spare[0], spare[1]

        item_rest = a_ring[:, 1:A_SLOTS, :].rearrange("p s n -> p (s n)")

        def item_cols(at, n):
            return y[:, at:at + n] if at < ITEM_Y else item_rest[:, at - ITEM_Y:at - ITEM_Y + n]

        piece_end = [min(N_ITEM, ITEM_Y + s * GROUP_W) for s in range(A_SLOTS)]

        bias_loaded = sem("bias_loaded")
        w_item_loaded = sem("w_item_loaded")
        user_loaded = sem("user_loaded")
        item_loaded = [sem(f"item_loaded{s}") for s in range(A_SLOTS)]
        a_loaded = [sem(f"a_loaded{s}") for s in range(A_SLOTS)]
        rows_loaded = sem("rows_loaded")
        ones_set = sem("ones_set")
        ones_r_set = sem("ones_r_set")
        take_zero = sem("take_zero")
        take_set = sem("take_set")
        ident_zero = sem("ident_zero")
        ident_set = sem("ident_set")
        bias_hi_set = sem("bias_hi_set")
        bias_set = sem("bias_set")
        quad_done = sem("quad_done")
        quad_hi = sem("quad_hi")
        quad_lo = sem("quad_lo")
        rem_set = sem("rem_set")
        hi_written = sem("hi_written")
        lo_written = [sem(f"lo_written{s}") for s in range(A_SLOTS)]
        chunk_used = [sem(f"chunk_used{s}") for s in range(S_SLOTS)]
        acc_done = sem("acc_done")
        y_ready = [sem(f"y_ready{k}") for k in range(ACC_BANKS)]
        stored = sem("stored")
        y_free = sem("y_free")
        chain = sem("chain")
        centred_ready = sem("centred_ready")
        squares_ready = sem("squares_ready")
        var_ready = sem("var_ready")
        half_set = sem("half_set")
        rstd_set = sem("rstd_set")
        std_ready = sem("std_ready")
        normed_ready = sem("normed_ready")
        turned_ready = sem("turned_ready")
        normed_t_ready = sem("normed_t_ready")
        y_holds_x = sem("y_holds_x")

        block = ctx.enter_context(nc.Block())

        @block.sync
        def _(sp):
            for free in (*lo_written, acc_done):
                sp.sem_inc(free, FREE)
            sp.dma_start(wi[:, :], w_item_t).then_inc(w_item_loaded, 16)
            sp.dma_start(bi[:, :], b_item).then_inc(bias_loaded, 16)
            for s in range(A_SLOTS):
                at = 0 if s == 0 else piece_end[s - 1]
                sp.dma_start(item_cols(at, piece_end[s] - at), item_t[:, at:piece_end[s]]).then_inc(item_loaded[s], 16)
            sp.dma_start(wu[:, :], w_user_t).then_inc(user_loaded, 16)
            sp.dma_start(h_rem[REM:REM + 1, :], b_user).then_inc(user_loaded, 16)

            def load(g, c, s, turn):
                splits, tile = sp.snap(g * LOADS[s] + (turn + FREE)), sp.snap(g * CHUNKS + c)
                if s == REM_SLOT:
                    sp.wait_ge(acc_done, sp.snap(g * ACC_BANKS + FREE))
                sp.wait_ge(lo_written[s], splits)
                if s > 0:
                    sp.wait_ge(quad_done, -(-piece_end[s] // (QUAD * P)))
                sp.dma_start(a_ring[:, s, :], adj_tiles[bass.ds(tile, 1), :, :].rearrange("o p n -> (o p) n")).then_inc(a_loaded[s], 16)

            with sp.Fori(0, GROUPS) as g:
                with sp.Fori(0, CHUNKS // A_SLOTS) as turn:
                    for s in range(A_SLOTS):
                        load(g, turn * A_SLOTS + s, s, turn)
                for s in range(REM_SLOT):
                    load(g, CHUNKS // A_SLOTS * A_SLOTS + s, s, CHUNKS // A_SLOTS)
                sp.wait_ge(lo_written[REM_SLOT], g * LOADS[REM_SLOT] + (LOADS[REM_SLOT] + FREE))
                sp.dma_start(a_ring[0:REM, REM_SLOT, :], adj_rem[bass.ds(g, 1), :, :].rearrange("o p n -> (o p) n")).then_inc(a_loaded[REM_SLOT], 16)
                sp.dma_start(a_ring[REM:REM + 1, REM_SLOT, :], ones_row).then_inc(a_loaded[REM_SLOT], 16)

        signals = [LOADS[s] + (2 if s == REM_SLOT else 0) for s in range(A_SLOTS)]

        @block.gpsimd
        def _(pool):
            nc.gpsimd.memset(take_hi[:, :], 0.0).then_inc(take_zero, 1)
            pool.wait_ge(take_zero, 1)
            nc.gpsimd.affine_select(out=take_hi[:, :], in_=take_hi[:, :], compare_op=ALU.not_equal, fill=-1.0, base=-1,
                                    pattern=[[0, 1]], channel_multiplier=1).then_inc(take_set, 1)
            nc.gpsimd.memset(ident[:, :], 0.0).then_inc(ident_zero, 1)
            pool.wait_ge(ident_zero, 1)
            nc.gpsimd.affine_select(out=ident[:, :], in_=ident[:, :], compare_op=ALU.not_equal, fill=1.0, base=0,
                                    pattern=[[-1, ROW_T]], channel_multiplier=1).then_inc(ident_set, 1)
            pool.sem_inc(turned_ready, FREE)

            with pool.Fori(0, GROUPS) as g:
                with pool.Fori(0, UNITS) as k:
                    pool.wait_ge(turned_ready, g * UNITS + k + FREE)
                    pool.dma_start(rows[:, :, :], x_rows[bass.ds(g * UNITS + k, 1), :, :, :].rearrange("o p t c -> (o p) t c")).then_inc(rows_loaded, 16)
                for k in range(ACC_BANKS):
                    pool.wait_ge(y_ready[k], g + (1 + FREE))
                    pool.dma_start(out_t[bass.ds(g, 1), :, k * BANK_W:(k + 1) * BANK_W].rearrange("o p n -> (o p) n"), y[:, k * BANK_W:(k + 1) * BANK_W]).then_inc(stored, 16)
                pool.wait_ge(stored, g * (16 * ACC_BANKS) + 16 * ACC_BANKS)
                pool.sem_inc(y_free, 1)

        @block.scalar
        def _(act):
            for free in (*chunk_used, y_free):
                act.sem_inc(free, FREE)
            act.wait_ge(bias_loaded, 16)
            nc.scalar.copy(bi_hi[:, :], bi[:, :]).then_inc(bias_hi_set, 1)
            act.wait_ge(ones_set, 1)
            nc.scalar.copy(ones_r[:, :], ones_f[:, :]).then_inc(ones_r_set, 1)

            def round_hi(g, c0, it=0):
                s, r = c0 % A_SLOTS, c0 % S_SLOTS
                act.wait_ge(a_loaded[s], (g * signals[s] + it * (BODY // A_SLOTS) + (c0 // A_SLOTS + 1)) * 16)
                act.wait_ge(chunk_used[r], g * SPLITS + it * (BODY // S_SLOTS) + (c0 // S_SLOTS + FREE))
                nc.scalar.copy(hi_ring[:, r, :], a_ring[:, s, :]).then_inc(hi_written, 1)

            for q in range(QUADS):
                full = min(QUAD, CHUNKS - q * QUAD)
                act.wait_ge(quad_done, q + 1)
                bank = spare[q % H_BANKS]
                if q == QUADS - 1:
                    nc.scalar.copy(h_rem[0:REM, :], bank[0:REM, full * HID:(full + 1) * HID]).then_inc(rem_set, 1)
                nc.scalar.copy(h_hi[:, q * QUAD:q * QUAD + full, :],
                               bank[:, 0:full * HID].rearrange("p (c d) -> p c d", d=HID)).then_inc(quad_hi, 1)
                if q in EARLY:
                    round_hi(0, EARLY[q])

            def group(g):
                for c in range(AHEAD, SCALAR_LOOP_AT):
                    round_hi(g, c)
                with act.Fori(0, UNITS) as k:
                    for at in range(SCALAR_LOOP_AT, SCALAR_LOOP_AT + BODY):
                        round_hi(g, at, k)
                        if at == SQUARE_AT:
                            act.wait_ge(centred_ready, g * UNITS + k + 1)
                            nc.scalar.activation(squares[:, :, :], centred[:, :, :], ACT.Square).then_inc(squares_ready, 1)
                        if at == SQRT_AT:
                            act.wait_ge(var_ready, g * UNITS + k + 1)
                            nc.scalar.activation(std, var, ACT.Sqrt).then_inc(std_ready, 1)
                        if at == COPY_AT:
                            act.wait_ge(turned_ready, g * UNITS + k + (1 + FREE))
                            nc.scalar.copy(normed_t[:, :], turned[:, 0:BANK_W]).then_inc(normed_t_ready, 1)
                            act.wait_ge(y_free, g + FREE)
                            nc.scalar.copy(y[:, bass.ds(k * BANK_W, BANK_W)], turned_x[:, 0:BANK_W]).then_inc(y_holds_x, 1)
                for c in range(SCALAR_LOOP_AT + BODY * UNITS, CHUNKS):
                    round_hi(g, c)

            with act.Fori(0, GROUPS - 1) as g:
                group(g)
                for c in range(AHEAD):
                    round_hi(g + 1, c)
            group(GROUPS - 1)

        @block.vector
        def _(dve):
            nc.vector.memset(ones_f[:, :], 1.0).then_inc(ones_set, 1)
            dve.wait_ge(bias_hi_set, 1)
            dve.wait_ge(take_set, 1)
            nc.vector.scalar_tensor_tensor(out=bi_parts[:, :], in0=bi_hi[:, :], scalar=take_hi[:, 0:1], in1=bi[:, :],
                                           op0=ALU.mult, op1=ALU.add).then_inc(bias_set, 1)

            def subtract_lo(g, c0, it=0):
                s, r = c0 % A_SLOTS, c0 % S_SLOTS
                dve.wait_ge(hi_written, g * CHUNKS + it * BODY + (c0 + 1))
                nc.vector.tensor_tensor(lo_ring[:, r, :], a_ring[:, s, :], hi_ring[:, r, :], ALU.subtract).then_inc(lo_written[s], 1)

            for q in range(QUADS):
                full = min(QUAD, CHUNKS - q * QUAD)
                dve.wait_ge(quad_hi, q + 1)
                nc.vector.tensor_tensor(h_lo[:, q * QUAD:q * QUAD + full, :],
                                        spare[q % H_BANKS][:, 0:full * HID].rearrange("p (c d) -> p c d", d=HID),
                                        h_hi[:, q * QUAD:q * QUAD + full, :], ALU.subtract).then_inc(quad_lo, 1)
                if q in EARLY:
                    subtract_lo(0, EARLY[q])

            steps = 6
            wide = [ROW_T, ROW_TILES, HID]

            def centre(u):
                dve.wait_ge(rows_loaded, u * 16 + 16)
                nc.vector.reduce_sum(total, rows[:, :, :], AX_X).then_inc(chain, 1)
                dve.wait_ge(chain, u * steps + 1)
                nc.vector.tensor_scalar(mean, total, 1.0 / HID, None, ALU.mult).then_inc(chain, 1)
                dve.wait_ge(chain, u * steps + 2)
                nc.vector.tensor_tensor(centred[:, :, :], rows[:, :, :], mean.unsqueeze(2).broadcast_to(wide),
                                        ALU.subtract).then_inc(centred_ready, 1)

            def variance(u):
                dve.wait_ge(squares_ready, u + 1)
                nc.vector.reduce_sum(total_sq, squares[:, :, :], AX_X).then_inc(chain, 1)
                dve.wait_ge(chain, u * steps + 3)
                nc.vector.tensor_scalar(var, total_sq, 1.0 / HID, EPS, ALU.mult, ALU.add).then_inc(var_ready, 1)

            def norm(u):
                dve.wait_ge(std_ready, u + 1)
                nc.vector.reciprocal(inv, std).then_inc(chain, 1)
                dve.wait_ge(chain, u * steps + 4)
                nc.vector.tensor_tensor(root, inv, var, ALU.mult).then_inc(chain, 1)
                dve.wait_ge(chain, u * steps + 5)
                nc.vector.tensor_tensor(inv, root, std, ALU.add).then_inc(chain, 1)
                dve.wait_ge(chain, u * steps + 6)
                nc.vector.tensor_scalar(root, inv, 0.5, None, ALU.mult).then_inc(half_set, 1)
                dve.wait_ge(half_set, u + 1)
                nc.vector.reciprocal(rstd, root).then_inc(rstd_set, 1)
                dve.wait_ge(rstd_set, u + 1)
                nc.vector.scalar_tensor_tensor(out=normed[:, :, :], in0=centred[:, :, :], scalar=0.0,
                                               in1=rstd.unsqueeze(2).broadcast_to(wide), op0=ALU.max,
                                               op1=ALU.mult).then_inc(normed_ready, 1)

            def empty(g):
                dve.wait_ge(y_holds_x, g * UNITS + UNITS)
                for k in range(ACC_BANKS):
                    cols = y[:, k * BANK_W:(k + 1) * BANK_W]
                    dve.wait_ge(acc_done, g * ACC_BANKS + (k + 1 + FREE))
                    nc.vector.scalar_tensor_tensor(out=cols, in0=acc[k][:, 0:BANK_W], scalar=0.0, in1=cols,
                                                   op0=ALU.max, op1=ALU.add).then_inc(y_ready[k], 1)

            def group(g):
                with dve.Fori(0, UNITS) as k:
                    for at in range(VECTOR_LOOP_AT, VECTOR_LOOP_AT + BODY):
                        subtract_lo(g, at, k)
                        if at == CENTRE_AT:
                            centre(g * UNITS + k)
                        if at == VAR_AT:
                            variance(g * UNITS + k)
                        if at == NORM_AT:
                            norm(g * UNITS + k)
                for c in range(VECTOR_LOOP_AT + BODY * UNITS, CHUNKS):
                    subtract_lo(g, c)

            with dve.Fori(0, GROUPS - 1) as g:
                group(g)
                for c in range(AHEAD):
                    subtract_lo(g + 1, c)
                empty(g)
            group(GROUPS - 1)
            empty(GROUPS - 1)

        @block.tensor
        def _(pe):
            for free in y_ready:
                pe.sem_inc(free, FREE)
            pe.wait_ge(w_item_loaded, 16)
            pe.wait_ge(ones_r_set, 1)
            pe.wait_ge(bias_set, 1)
            for q in range(QUADS):
                cols = min(N_ITEM - q * QUAD * P, QUAD * P)
                parts = -(-cols // P)
                pe.wait_ge(item_loaded[next(s for s in range(A_SLOTS) if q * QUAD * P + cols <= piece_end[s])], 16)
                if q >= H_BANKS:
                    pe.wait_ge(quad_lo, q - H_BANKS + 1)
                bank = spare[q % H_BANKS]
                nc.tensor.matmul(bank[:, 0:parts * HID].rearrange("p (c d) -> p c d", d=HID), ones_r[:, :],
                                 bi_parts[:, :].unsqueeze(1).broadcast_to([2, parts, HID]),
                                 start=True, stop=False, skip_group_check=True)
                for m in range(parts):
                    n = min(P, cols - m * P)
                    at = (q * QUAD + m) * P
                    last = nc.tensor.matmul(bank[0:n, m * HID:(m + 1) * HID], item_cols(at, n), wi[:, :],
                                            start=False, stop=True, skip_group_check=True)
                last.then_inc(quad_done, 1)
            pe.wait_ge(quad_lo, QUADS)
            pe.wait_ge(rem_set, 1)
            pe.wait_ge(ident_set, 1)
            pe.wait_ge(user_loaded, 32)

            with pe.Fori(0, GROUPS) as g:
                for c in range(CHUNKS):
                    s, r = c % A_SLOTS, c % S_SLOTS
                    k = (c - TRANSPOSE_AT) // BODY
                    if c == TRANSPOSE_AT + BODY * k and 0 <= k < UNITS:
                        pe.wait_ge(normed_ready, g * UNITS + k + 1)
                        for t in range(ROW_TILES):
                            nc.tensor.transpose(turned_x[:, t * ROW_T:(t + 1) * ROW_T], rows[:, t, :], ident[:, :])
                        for t in range(ROW_TILES):
                            last = nc.tensor.transpose(turned[:, t * ROW_T:(t + 1) * ROW_T], normed[:, t, :], ident[:, :])
                        last.then_inc(turned_ready, 1)
                    k = (c - USER_AT) // BODY
                    if c == USER_AT + BODY * k and 0 <= k < UNITS:
                        pe.wait_ge(normed_t_ready, g * UNITS + k + 1)
                        nc.tensor.matmul(acc[k][:, 0:BANK_W], wu[:, :], normed_t[:, :], start=False, stop=False,
                                         skip_group_check=True)
                    pe.wait_ge(hi_written, g * CHUNKS + (c + 1))
                    for h_part in (h_lo, h_hi):
                        for k in range(ACC_BANKS):
                            if c == 0 and h_part is h_lo:
                                pe.wait_ge(y_ready[k], g + FREE)
                            nc.tensor.matmul(acc[k][:, 0:BANK_W], h_part[:, c, :],
                                             hi_ring[:, r, k * BANK_W:(k + 1) * BANK_W],
                                             start=(c == 0 and h_part is h_lo), stop=False, skip_group_check=True)
                    pe.wait_ge(lo_written[s], g * LOADS[s] + (c // A_SLOTS + 1 + FREE))
                    for k in range(ACC_BANKS):
                        last = nc.tensor.matmul(acc[k][:, 0:BANK_W], h_hi[:, c, :],
                                                lo_ring[:, r, k * BANK_W:(k + 1) * BANK_W],
                                                start=False, stop=False, skip_group_check=True)
                    last.then_inc(chunk_used[r], 1)
                pe.wait_ge(a_loaded[REM_SLOT], g * (signals[REM_SLOT] * 16) + signals[REM_SLOT] * 16)
                for k in range(ACC_BANKS):
                    nc.tensor.matmul(acc[k][:, 0:BANK_W], h_rem[:, :],
                                     a_ring[0:REM + 1, REM_SLOT, k * BANK_W:(k + 1) * BANK_W],
                                     start=False, stop=True, skip_group_check=True).then_inc(acc_done, 1)


def kernel(x, adj, L0_gnn_item_feat, L0_gnn_W_item, L0_gnn_b_item, L0_gnn_W_user, L0_gnn_b_user):
    import numpy as np
    import concourse.bacc as bacc
    from concourse.bass_utils import run_bass_kernel_spmd

    x, adj = np.asarray(x), np.asarray(adj)
    full = CHUNKS * P
    arrays = {
        "adj_tiles": adj[:, :full].reshape(GROUPS, GROUP_W, CHUNKS, P).transpose(0, 2, 3, 1).reshape(GROUPS * CHUNKS, P, GROUP_W),
        "adj_rem": adj[:, full:].reshape(GROUPS, GROUP_W, REM).transpose(0, 2, 1),
        "ones_row": np.ones((1, GROUP_W), np.float32),
        "item_t": np.asarray(L0_gnn_item_feat).T,
        "x_rows": x.reshape(GROUPS * UNITS, ROW_TILES, ROW_T, HID).transpose(0, 2, 1, 3),
        "w_item_t": np.asarray(L0_gnn_W_item).T,
        "b_item": np.tile(np.asarray(L0_gnn_b_item), 2).reshape(2, HID),
        "w_user_t": np.asarray(L0_gnn_W_user).T,
        "b_user": np.asarray(L0_gnn_b_user).reshape(1, HID),
    }
    nc = bacc.Bacc("TRN2", target_bir_lowering=False, num_devices=1)
    given, args = {}, []
    for name, a in arrays.items():
        a = np.ascontiguousarray(a)
        given[f"in_{name}"] = a
        args.append(nc.dram_tensor(f"in_{name}", a.shape, mybir.dt.from_np(a.dtype), kind="ExternalInput").ap())
    out_t = nc.dram_tensor("out_t", (GROUPS, HID, GROUP_W), F32, kind="ExternalOutput").ap()
    graph_layer(nc, *args, out_t)
    r = run_bass_kernel_spmd(nc, [given], core_ids=[0])
    return np.ascontiguousarray(r.results[0]["out_t"].transpose(0, 2, 1).reshape(N_USER, HID))
```

```python
from contextlib import ExitStack

import concourse.bass as bass
from concourse import mybir

P = 128
N_USER = 10000
N_ITEM = 10000
HID = 128
EPS = 1e-5

GROUPS = 5
ACC_BANKS = 4
GROUP_W = N_USER // GROUPS
BANK_W = GROUP_W // ACC_BANKS
PITCH = -(-GROUP_W // 64) * 64
ROW_TILES = 4
ROW_T = BANK_W // ROW_TILES

CHUNKS = N_ITEM // P
REM = N_ITEM - CHUNKS * P
A_SLOTS = 6
S_SLOTS = 3
BODY = 12
LOADS = CHUNKS // A_SLOTS
SPLITS = CHUNKS // S_SLOTS
ROWS_BLOCK = 32
REM_AFTER = 2

QUAD = 4
QUADS = -(-N_ITEM // (QUAD * P))
H_BANKS = 4
ITEM_Y = 4 * QUAD * P
ITEM_SLOT = 2
ITEM_PIECES = 1 + A_SLOTS - ITEM_SLOT
UNITS = ACC_BANKS
FREE = 1

assert GROUP_W * GROUPS == N_USER and BANK_W * ACC_BANKS == GROUP_W and BANK_W <= 512
assert CHUNKS % S_SLOTS == 0 and CHUNKS % A_SLOTS == 0 and BODY % A_SLOTS == 0 and BODY % S_SLOTS == 0
assert ITEM_Y + (ITEM_PIECES - 2) * PITCH < N_ITEM <= ITEM_Y + (ITEM_PIECES - 1) * PITCH
assert REM < ROWS_BLOCK and ACC_BANKS * ROWS_BLOCK <= P

F32 = mybir.dt.float32
F32R = mybir.dt.float32r
ALU = mybir.AluOpType
ACT = mybir.ActivationFunctionType
AX_X = mybir.AxisListType.X

CENTRE_AT = 4
SQUARE_AT = 7
VAR_AT = 8
SQRT_AT = 11
NORM_AT = 12
TURN_X_AT = 7
TRANSPOSE_AT = 14
COPY_AT = 17
USER_AT = 18
AHEAD = 2
VECTOR_LOOP_AT = 2
SCALAR_LOOP_AT = 6
EARLY = {12: 0, 15: 1}


def graph_layer(nc, adj_tiles, adj_rem, ones_row, item_t, x_rows, w_item_t, b_item, w_user_t, b_user, out_t):
    with ExitStack() as ctx:
        def sb(name, shape, dt=F32):
            return ctx.enter_context(nc.sbuf_tensor(name, shape, dt))

        def sem(name):
            return ctx.enter_context(nc.semaphore(name))

        a_ring = sb("a_ring", [P, A_SLOTS, PITCH])
        hi_ring = sb("hi_ring", [P, S_SLOTS, GROUP_W], F32R)
        lo_ring = sb("lo_ring", [P, S_SLOTS, GROUP_W], F32R)
        h_hi = sb("h_hi", [P, CHUNKS, HID], F32R)
        h_lo = sb("h_lo", [P, CHUNKS, HID], F32R)
        a_rem = sb("a_rem", [P, BANK_W])
        h_rem = sb("h_rem", [P, HID])
        wi = sb("wi", [P, HID])
        wu = sb("wu", [P, HID])
        bi = sb("bi", [2, HID])
        bi_hi = sb("bi_hi", [2, HID], F32R)
        bi_parts = sb("bi_parts", [2, HID], F32R)
        ones_f = sb("ones_f", [2, P])
        ones_r = sb("ones_r", [2, P], F32R)
        take_hi = sb("take_hi", [2, 1])
        ident = sb("ident", [ROW_T, ROW_T])
        y = sb("y", [P, max(GROUP_W, ITEM_Y)])
        rows = sb("rows", [ROW_T, ROW_TILES, HID])
        centred = sb("centred", [ROW_T, ROW_TILES, HID])
        squares = sb("squares", [ROW_T, ROW_TILES, HID])
        normed = sb("normed", [ROW_T, ROW_TILES, HID])
        normed_t = sb("normed_t", [P, BANK_W])
        stat = sb("stat", [ROW_T, 8, ROW_TILES])
        total, mean, total_sq, var, std, inv, root, rstd = (stat[:, i, :] for i in range(8))

        acc = [ctx.enter_context(nc.psum_tensor(f"acc{k}", [P, 512], F32)) for k in range(ACC_BANKS)]
        spare = [ctx.enter_context(nc.psum_tensor(f"spare{k}", [P, 512], F32)) for k in range(H_BANKS)]
        turned, turned_x = spare[0], spare[1]

        item_rest = a_ring[:, ITEM_SLOT:A_SLOTS, :].rearrange("p s n -> p (s n)")

        def item_cols(at, n):
            return y[:, at:at + n] if at < ITEM_Y else item_rest[:, at - ITEM_Y:at - ITEM_Y + n]

        assert item_rest.shape[1] >= N_ITEM - ITEM_Y

        piece_end = [min(N_ITEM, ITEM_Y + i * PITCH) for i in range(ITEM_PIECES)]

        bias_loaded = sem("bias_loaded")
        w_item_loaded = sem("w_item_loaded")
        user_loaded = sem("user_loaded")
        item_loaded = [sem(f"item_loaded{i}") for i in range(ITEM_PIECES)]
        a_loaded = [sem(f"a_loaded{s}") for s in range(A_SLOTS)]
        rem_loaded = sem("rem_loaded")
        ones_loaded = sem("ones_loaded")
        rows_loaded = sem("rows_loaded")
        ones_set = sem("ones_set")
        ones_r_set = sem("ones_r_set")
        take_zero = sem("take_zero")
        take_set = sem("take_set")
        ident_zero = sem("ident_zero")
        ident_set = sem("ident_set")
        bias_hi_set = sem("bias_hi_set")
        bias_set = sem("bias_set")
        quad_done = sem("quad_done")
        quad_hi = sem("quad_hi")
        quad_lo = sem("quad_lo")
        rem_set = sem("rem_set")
        hi_written = sem("hi_written")
        lo_written = [sem(f"lo_written{s}") for s in range(A_SLOTS)]
        chunk_used = [sem(f"chunk_used{s}") for s in range(S_SLOTS)]
        acc_done = sem("acc_done")
        y_ready = [sem(f"y_ready{k}") for k in range(ACC_BANKS)]
        stored = sem("stored")
        last_stored = sem("last_stored")
        y_free = sem("y_free")
        chain = sem("chain")
        centred_ready = sem("centred_ready")
        squares_ready = sem("squares_ready")
        var_ready = sem("var_ready")
        half_set = sem("half_set")
        rstd_set = sem("rstd_set")
        std_ready = sem("std_ready")
        normed_ready = sem("normed_ready")
        x_turned = sem("x_turned")
        turned_ready = sem("turned_ready")
        normed_t_ready = sem("normed_t_ready")
        y_holds_x = sem("y_holds_x")

        block = ctx.enter_context(nc.Block())

        @block.sync
        def _(sp):
            for free in (*lo_written, acc_done):
                sp.sem_inc(free, FREE)
            sp.dma_start(wi[:, :], w_item_t).then_inc(w_item_loaded, 16)
            sp.dma_start(bi[:, :], b_item).then_inc(bias_loaded, 16)
            for i in range(ITEM_PIECES):
                at = 0 if i == 0 else piece_end[i - 1]
                sp.dma_start(item_cols(at, piece_end[i] - at), item_t[:, at:piece_end[i]]).then_inc(item_loaded[i], 16)
            sp.dma_start(wu[:, :], w_user_t).then_inc(user_loaded, 16)
            for k in range(ACC_BANKS):
                row = k * ROWS_BLOCK + REM
                sp.dma_start(h_rem[row:row + 1, :], b_user).then_inc(user_loaded, 16)
                sp.dma_start(a_rem[row:row + 1, :], ones_row).then_inc(ones_loaded, 16)

            def turn_of_ring(g, turn):
                for s in range(A_SLOTS):
                    splits, tile = sp.snap(g * LOADS + (turn + FREE)), sp.snap(g * CHUNKS + (turn * A_SLOTS + s))
                    sp.wait_ge(lo_written[s], splits)
                    if s >= ITEM_SLOT:
                        sp.wait_ge(quad_done, -(-piece_end[s - ITEM_SLOT + 1] // (QUAD * P)))
                    sp.dma_start(a_ring[:, s, 0:GROUP_W], adj_tiles[bass.ds(tile, 1), :, 0:GROUP_W].rearrange("o p n -> (o p) n")).then_inc(a_loaded[s], 16)

            with sp.Fori(0, GROUPS) as g:
                with sp.Fori(0, REM_AFTER) as turn:
                    turn_of_ring(g, turn)
                sp.wait_ge(acc_done, g * ACC_BANKS + FREE)
                for k in range(ACC_BANKS):
                    row = k * ROWS_BLOCK
                    sp.dma_start(a_rem[row:row + REM, :], adj_rem[bass.ds(g * ACC_BANKS + k, 1), :, :].rearrange("o p n -> (o p) n")).then_inc(rem_loaded, 16)
                with sp.Fori(REM_AFTER, LOADS) as turn:
                    turn_of_ring(g, turn)
            for k in range(ACC_BANKS):
                sp.wait_ge(y_ready[k], GROUPS + FREE)
                sp.dma_start(out_t[GROUPS - 1, :, k * BANK_W:(k + 1) * BANK_W], y[:, k * BANK_W:(k + 1) * BANK_W]).then_inc(last_stored, 16)
            sp.wait_ge(last_stored, 16 * ACC_BANKS)

        @block.gpsimd
        def _(pool):
            nc.gpsimd.memset(take_hi[:, :], 0.0).then_inc(take_zero, 1)
            pool.wait_ge(take_zero, 1)
            nc.gpsimd.affine_select(out=take_hi[:, :], in_=take_hi[:, :], compare_op=ALU.not_equal, fill=-1.0, base=-1,
                                    pattern=[[0, 1]], channel_multiplier=1).then_inc(take_set, 1)
            nc.gpsimd.memset(ident[:, :], 0.0).then_inc(ident_zero, 1)
            pool.wait_ge(ident_zero, 1)
            nc.gpsimd.affine_select(out=ident[:, :], in_=ident[:, :], compare_op=ALU.not_equal, fill=1.0, base=0,
                                    pattern=[[-1, ROW_T]], channel_multiplier=1).then_inc(ident_set, 1)

            def load_rows(u):
                pool.dma_start(rows[:, :, :], x_rows[bass.ds(u, 1), :, :, :].rearrange("o p t c -> (o p) t c")).then_inc(rows_loaded, 16)

            def load_rows_after(g, k):
                pool.wait_ge(x_turned, g * UNITS + k)
                load_rows(g * UNITS + k)

            load_rows(0)
            with pool.Fori(0, GROUPS - 1) as g:
                with pool.Fori(1, UNITS + 1) as k:
                    load_rows_after(g, k)
                for k in range(ACC_BANKS):
                    pool.wait_ge(y_ready[k], g + (1 + FREE))
                    pool.dma_start(out_t[bass.ds(g, 1), :, k * BANK_W:(k + 1) * BANK_W].rearrange("o p n -> (o p) n"), y[:, k * BANK_W:(k + 1) * BANK_W]).then_inc(stored, 16)
                pool.wait_ge(stored, g * (16 * ACC_BANKS) + 16 * ACC_BANKS)
                pool.sem_inc(y_free, 1)
            with pool.Fori(1, UNITS) as k:
                load_rows_after(GROUPS - 1, k)

        @block.scalar
        def _(act):
            for free in (*chunk_used, y_free):
                act.sem_inc(free, FREE)
            act.wait_ge(bias_loaded, 16)
            nc.scalar.copy(bi_hi[:, :], bi[:, :]).then_inc(bias_hi_set, 1)
            act.wait_ge(ones_set, 1)
            nc.scalar.copy(ones_r[:, :], ones_f[:, :]).then_inc(ones_r_set, 1)

            def round_hi(g, c0, it=0):
                s, r = c0 % A_SLOTS, c0 % S_SLOTS
                act.wait_ge(a_loaded[s], (g * LOADS + it * (BODY // A_SLOTS) + (c0 // A_SLOTS + 1)) * 16)
                act.wait_ge(chunk_used[r], g * SPLITS + it * (BODY // S_SLOTS) + (c0 // S_SLOTS + FREE))
                nc.scalar.copy(hi_ring[:, r, :], a_ring[:, s, 0:GROUP_W]).then_inc(hi_written, 1)

            for q in range(QUADS):
                full = min(QUAD, CHUNKS - q * QUAD)
                act.wait_ge(quad_done, q + 1)
                bank = spare[q % H_BANKS]
                if q == QUADS - 1:
                    for k in range(ACC_BANKS):
                        row = k * ROWS_BLOCK
                        nc.scalar.copy(h_rem[row:row + REM, :], bank[0:REM, full * HID:(full + 1) * HID]).then_inc(rem_set, 1)
                nc.scalar.copy(h_hi[:, q * QUAD:q * QUAD + full, :],
                               bank[:, 0:full * HID].rearrange("p (c d) -> p c d", d=HID)).then_inc(quad_hi, 1)
                if q in EARLY:
                    round_hi(0, EARLY[q])

            def group(g):
                for c in range(AHEAD, SCALAR_LOOP_AT):
                    round_hi(g, c)
                with act.Fori(0, UNITS) as k:
                    for at in range(SCALAR_LOOP_AT, SCALAR_LOOP_AT + BODY):
                        round_hi(g, at, k)
                        if at == SQUARE_AT:
                            act.wait_ge(centred_ready, g * UNITS + k + 1)
                            nc.scalar.activation(squares[:, :, :], centred[:, :, :], ACT.Square).then_inc(squares_ready, 1)
                        if at == SQRT_AT:
                            act.wait_ge(var_ready, g * UNITS + k + 1)
                            nc.scalar.activation(std, var, ACT.Sqrt).then_inc(std_ready, 1)
                        if at == COPY_AT:
                            act.wait_ge(y_free, g + FREE)
                            act.wait_ge(x_turned, g * UNITS + k + 1)
                            nc.scalar.copy(y[:, bass.ds(k * BANK_W, BANK_W)], turned_x[:, 0:BANK_W]).then_inc(y_holds_x, 1)
                            act.wait_ge(turned_ready, g * UNITS + k + 1)
                            nc.scalar.copy(normed_t[:, :], turned[:, 0:BANK_W]).then_inc(normed_t_ready, 1)
                for c in range(SCALAR_LOOP_AT + BODY * UNITS, CHUNKS):
                    round_hi(g, c)

            with act.Fori(0, GROUPS - 1) as g:
                group(g)
                for c in range(AHEAD):
                    round_hi(g + 1, c)
            group(GROUPS - 1)

        @block.vector
        def _(dve):
            nc.vector.memset(ones_f[:, :], 1.0).then_inc(ones_set, 1)
            dve.wait_ge(bias_hi_set, 1)
            dve.wait_ge(take_set, 1)
            nc.vector.scalar_tensor_tensor(out=bi_parts[:, :], in0=bi_hi[:, :], scalar=take_hi[:, 0:1], in1=bi[:, :],
                                           op0=ALU.mult, op1=ALU.add).then_inc(bias_set, 1)

            def subtract_lo(g, c0, it=0):
                s, r = c0 % A_SLOTS, c0 % S_SLOTS
                dve.wait_ge(hi_written, g * CHUNKS + it * BODY + (c0 + 1))
                nc.vector.tensor_tensor(lo_ring[:, r, :], a_ring[:, s, 0:GROUP_W], hi_ring[:, r, :], ALU.subtract).then_inc(lo_written[s], 1)

            for q in range(QUADS):
                full = min(QUAD, CHUNKS - q * QUAD)
                dve.wait_ge(quad_hi, q + 1)
                nc.vector.tensor_tensor(h_lo[:, q * QUAD:q * QUAD + full, :],
                                        spare[q % H_BANKS][:, 0:full * HID].rearrange("p (c d) -> p c d", d=HID),
                                        h_hi[:, q * QUAD:q * QUAD + full, :], ALU.subtract).then_inc(quad_lo, 1)
                if q in EARLY:
                    subtract_lo(0, EARLY[q])

            steps = 6
            wide = [ROW_T, ROW_TILES, HID]

            def centre(u):
                dve.wait_ge(rows_loaded, u * 16 + 16)
                nc.vector.reduce_sum(total, rows[:, :, :], AX_X).then_inc(chain, 1)
                dve.wait_ge(chain, u * steps + 1)
                nc.vector.tensor_scalar(mean, total, 1.0 / HID, None, ALU.mult).then_inc(chain, 1)
                dve.wait_ge(chain, u * steps + 2)
                nc.vector.tensor_tensor(centred[:, :, :], rows[:, :, :], mean.unsqueeze(2).broadcast_to(wide),
                                        ALU.subtract).then_inc(centred_ready, 1)

            def variance(u):
                dve.wait_ge(squares_ready, u + 1)
                nc.vector.reduce_sum(total_sq, squares[:, :, :], AX_X).then_inc(chain, 1)
                dve.wait_ge(chain, u * steps + 3)
                nc.vector.tensor_scalar(var, total_sq, 1.0 / HID, EPS, ALU.mult, ALU.add).then_inc(var_ready, 1)

            def norm(u):
                dve.wait_ge(std_ready, u + 1)
                nc.vector.reciprocal(inv, std).then_inc(chain, 1)
                dve.wait_ge(chain, u * steps + 4)
                nc.vector.tensor_tensor(root, inv, var, ALU.mult).then_inc(chain, 1)
                dve.wait_ge(chain, u * steps + 5)
                nc.vector.tensor_tensor(inv, root, std, ALU.add).then_inc(chain, 1)
                dve.wait_ge(chain, u * steps + 6)
                nc.vector.tensor_scalar(root, inv, 0.5, None, ALU.mult).then_inc(half_set, 1)
                dve.wait_ge(half_set, u + 1)
                nc.vector.reciprocal(rstd, root).then_inc(rstd_set, 1)
                dve.wait_ge(rstd_set, u + 1)
                nc.vector.scalar_tensor_tensor(out=normed[:, :, :], in0=centred[:, :, :], scalar=0.0,
                                               in1=rstd.unsqueeze(2).broadcast_to(wide), op0=ALU.max,
                                               op1=ALU.mult).then_inc(normed_ready, 1)

            def empty(g):
                dve.wait_ge(y_holds_x, g * UNITS + UNITS)
                for k in range(ACC_BANKS):
                    cols = y[:, k * BANK_W:(k + 1) * BANK_W]
                    dve.wait_ge(acc_done, g * ACC_BANKS + (k + 1 + FREE))
                    nc.vector.scalar_tensor_tensor(out=cols, in0=acc[k][:, 0:BANK_W], scalar=0.0, in1=cols,
                                                   op0=ALU.max, op1=ALU.add).then_inc(y_ready[k], 1)

            def group(g):
                with dve.Fori(0, UNITS) as k:
                    for at in range(VECTOR_LOOP_AT, VECTOR_LOOP_AT + BODY):
                        subtract_lo(g, at, k)
                        if at == CENTRE_AT:
                            centre(g * UNITS + k)
                        if at == VAR_AT:
                            variance(g * UNITS + k)
                        if at == NORM_AT:
                            norm(g * UNITS + k)
                for c in range(VECTOR_LOOP_AT + BODY * UNITS, CHUNKS):
                    subtract_lo(g, c)

            with dve.Fori(0, GROUPS - 1) as g:
                group(g)
                for c in range(AHEAD):
                    subtract_lo(g + 1, c)
                empty(g)
            group(GROUPS - 1)
            empty(GROUPS - 1)

        @block.tensor
        def _(pe):
            for free in y_ready:
                pe.sem_inc(free, FREE)
            pe.wait_ge(w_item_loaded, 16)
            pe.wait_ge(ones_r_set, 1)
            pe.wait_ge(bias_set, 1)
            for q in range(QUADS):
                cols = min(N_ITEM - q * QUAD * P, QUAD * P)
                parts = -(-cols // P)
                pe.wait_ge(item_loaded[next(i for i in range(ITEM_PIECES) if q * QUAD * P + cols <= piece_end[i])], 16)
                if q >= H_BANKS:
                    pe.wait_ge(quad_lo, q - H_BANKS + 1)
                bank = spare[q % H_BANKS]
                nc.tensor.matmul(bank[:, 0:parts * HID].rearrange("p (c d) -> p c d", d=HID), ones_r[:, :],
                                 bi_parts[:, :].unsqueeze(1).broadcast_to([2, parts, HID]),
                                 start=True, stop=False, skip_group_check=True)
                for m in range(parts):
                    n = min(P, cols - m * P)
                    at = (q * QUAD + m) * P
                    last = nc.tensor.matmul(bank[0:n, m * HID:(m + 1) * HID], item_cols(at, n), wi[:, :],
                                            start=False, stop=True, skip_group_check=True)
                last.then_inc(quad_done, 1)
            pe.wait_ge(quad_lo, QUADS)
            pe.wait_ge(rem_set, ACC_BANKS)
            pe.wait_ge(ident_set, 1)
            pe.wait_ge(user_loaded, 16 + 16 * ACC_BANKS)
            pe.wait_ge(ones_loaded, 16 * ACC_BANKS)

            with nc.Fori(0, GROUPS, engines=[mybir.EngineType.PE], hint_back_edge=True) as g:
                for c in range(CHUNKS):
                    s, r = c % A_SLOTS, c % S_SLOTS
                    k = (c - TURN_X_AT) // BODY
                    if c == TURN_X_AT + BODY * k and 0 <= k < UNITS:
                        pe.wait_ge(centred_ready, g * UNITS + k + 1)
                        for t in range(ROW_TILES):
                            last = nc.tensor.transpose(turned_x[:, t * ROW_T:(t + 1) * ROW_T], rows[:, t, :], ident[:, :])
                        last.then_inc(x_turned, 1)
                    k = (c - TRANSPOSE_AT) // BODY
                    if c == TRANSPOSE_AT + BODY * k and 0 <= k < UNITS:
                        pe.wait_ge(normed_ready, g * UNITS + k + 1)
                        for t in range(ROW_TILES):
                            last = nc.tensor.transpose(turned[:, t * ROW_T:(t + 1) * ROW_T], normed[:, t, :], ident[:, :])
                        last.then_inc(turned_ready, 1)
                    k = (c - USER_AT) // BODY
                    if c == USER_AT + BODY * k and 0 <= k < UNITS:
                        pe.wait_ge(normed_t_ready, g * UNITS + k + 1)
                        nc.tensor.matmul(acc[k][:, 0:BANK_W], wu[:, :], normed_t[:, :], start=False, stop=False,
                                         skip_group_check=True)
                    pe.wait_ge(hi_written, g * CHUNKS + (c + 1))
                    for h_part in (h_lo, h_hi):
                        for k in range(ACC_BANKS):
                            if c == 0 and h_part is h_lo:
                                pe.wait_ge(y_ready[k], g + FREE)
                            nc.tensor.matmul(acc[k][:, 0:BANK_W], h_part[:, c, :],
                                             hi_ring[:, r, k * BANK_W:(k + 1) * BANK_W],
                                             start=(c == 0 and h_part is h_lo), stop=False, skip_group_check=True)
                    pe.wait_ge(lo_written[s], g * LOADS + (c // A_SLOTS + 1 + FREE))
                    for k in range(ACC_BANKS):
                        last = nc.tensor.matmul(acc[k][:, 0:BANK_W], h_hi[:, c, :],
                                                lo_ring[:, r, k * BANK_W:(k + 1) * BANK_W],
                                                start=False, stop=False, skip_group_check=True)
                    last.then_inc(chunk_used[r], 1)
                pe.wait_ge(rem_loaded, g * (16 * ACC_BANKS) + 16 * ACC_BANKS)
                for k in range(ACC_BANKS):
                    rows_k = slice(k * ROWS_BLOCK, k * ROWS_BLOCK + REM + 1)
                    nc.tensor.matmul(acc[k][:, 0:BANK_W], h_rem[rows_k, :], a_rem[rows_k, :],
                                     start=False, stop=True, skip_group_check=True).then_inc(acc_done, 1)


def kernel(x, adj, L0_gnn_item_feat, L0_gnn_W_item, L0_gnn_b_item, L0_gnn_W_user, L0_gnn_b_user):
    import numpy as np
    import concourse.bacc as bacc
    from concourse.bass_utils import run_bass_kernel_spmd

    x, adj = np.asarray(x), np.asarray(adj)
    full = CHUNKS * P
    adj_tiles = np.zeros((GROUPS, CHUNKS, P, PITCH), np.float32)
    adj_tiles[:, :, :, :GROUP_W] = adj[:, :full].reshape(GROUPS, GROUP_W, CHUNKS, P).transpose(0, 2, 3, 1)
    arrays = {
        "adj_tiles": adj_tiles.reshape(GROUPS * CHUNKS, P, PITCH),
        "adj_rem": adj[:, full:].reshape(GROUPS * ACC_BANKS, BANK_W, REM).transpose(0, 2, 1),
        "ones_row": np.ones((1, BANK_W), np.float32),
        "item_t": np.asarray(L0_gnn_item_feat).T,
        "x_rows": x.reshape(GROUPS * UNITS, ROW_TILES, ROW_T, HID).transpose(0, 2, 1, 3),
        "w_item_t": np.asarray(L0_gnn_W_item).T,
        "b_item": np.tile(np.asarray(L0_gnn_b_item), 2).reshape(2, HID),
        "w_user_t": np.asarray(L0_gnn_W_user).T,
        "b_user": np.asarray(L0_gnn_b_user).reshape(1, HID),
    }
    nc = bacc.Bacc("TRN2", target_bir_lowering=False, num_devices=1)
    given, args = {}, []
    for name, a in arrays.items():
        a = np.ascontiguousarray(a)
        given[f"in_{name}"] = a
        args.append(nc.dram_tensor(f"in_{name}", a.shape, mybir.dt.from_np(a.dtype), kind="ExternalInput").ap())
    out_t = nc.dram_tensor("out_t", (GROUPS, HID, GROUP_W), F32, kind="ExternalOutput").ap()
    graph_layer(nc, *args, out_t)
    r = run_bass_kernel_spmd(nc, [given], core_ids=[0])
    return np.ascontiguousarray(r.results[0]["out_t"].transpose(0, 2, 1).reshape(N_USER, HID))
```
